# Optimizing a Trainium2 kernel written in Bass

```python
import numpy as np
import jax
import jax.numpy as jnp

def _softmax(x, axis=-1):
    return jax.nn.softmax(x, axis=axis)

def _gelu(x):
    return jax.nn.gelu(x, approximate=True)

def _silu(x):
    return jax.nn.silu(x)

def _sigmoid(x):
    return jax.nn.sigmoid(x)

def _layernorm(x, axis=-1, eps=1e-05):
    m = jnp.mean(x, axis=axis, keepdims=True)
    v = jnp.var(x, axis=axis, keepdims=True)
    return (x - m) / jnp.sqrt(v + eps)

def _scatter_add(tgt, idx, src, axis=0):
    return tgt.at[idx].add(src)

def _segment_sum(src, seg, n):
    return jax.ops.segment_sum(src, seg, n)
kernel_name = 'mk_rec_standalone_d1_rec_r8_17ae1a'

def setup_inputs(seed: int=0):
    np.random.seed(seed)
    _w = jnp.asarray

    def _rec_inputs():
        import jax
        import jax.numpy as jnp
        _rk = jax.random.key(seed)
        r_x = -0.000104943 + 0.999951 * jax.random.normal(jax.random.fold_in(_rk, 1), (1024, 24, 1024), jnp.float32)
        return r_x
    r_x = _rec_inputs()

    def _L0_rec_setup():
        import jax, jax.numpy as jnp
        import numpy as np
        B = 1024
        T = 24
        S = 1024
        key = jax.random.key(seed)
        k1, k2, k3, k4, k5 = jax.random.split(key, 5)
        x = jax.random.normal(k1, (B, T, S), dtype=jnp.float32)
        W1 = jax.random.normal(k2, (S, T), dtype=jnp.float32) * (1.0 / np.sqrt(T))
        b1 = jax.random.normal(k3, (S,), dtype=jnp.float32) * 0.01
        W2 = jax.random.normal(k4, (S, S), dtype=jnp.float32) * (1.0 / np.sqrt(S))
        b2 = jax.random.normal(k5, (S,), dtype=jnp.float32) * 0.01
        return {'x': x, 'W1': W1, 'b1': b1, 'W2': W2, 'b2': b2}
    _L0_rec_all = _L0_rec_setup()
    _L0_rec_in = {k: v for k, v in _L0_rec_all.items() if k in ('W1', 'b1', 'W2', 'b2')}
    del _L0_rec_all
    return {'r_x': r_x, 'L0_rec_W1': _L0_rec_in['W1'], 'L0_rec_b1': _L0_rec_in['b1'], 'L0_rec_W2': _L0_rec_in['W2'], 'L0_rec_b2': _L0_rec_in['b2']}

def reference(r_x, L0_rec_W1, L0_rec_b1, L0_rec_W2, L0_rec_b2):
    import jax
    import jax.numpy as jnp

    def _L0_rec_ref(x, W1, b1, W2, b2):
        import jax, jax.numpy as jnp
        import numpy as np
        B = 1024
        T = 24
        S = 1024
        h = jax.nn.sigmoid(jnp.einsum('bts,st->bs', x, W1) + b1)
        return h @ W2.T + b2
    y = _L0_rec_ref(r_x, L0_rec_W1, L0_rec_b1, L0_rec_W2, L0_rec_b2)
    return y

_drawn_inputs = setup_inputs


def setup_inputs(seed=0):
    import zlib

    import numpy as np

    out = dict(_drawn_inputs(seed))
    spreads = {}
    factors = {'L0_rec_b1': 8.0, 'L0_rec_b2': 3.149}
    for name, (base, spread) in spreads.items():
        noise = np.random.default_rng([zlib.crc32(name.encode()), seed]).standard_normal(out[name].shape)
        drawn = base * np.exp(spread * noise) if base else spread * noise
        out[name] = jnp.asarray(drawn.astype(out[name].dtype))
    for name, factor in factors.items():
        out[name] = (out[name] * factor).astype(out[name].dtype)
    return out
```

```python
from contextlib import ExitStack

import concourse.bass as bass
from concourse import mybir

F32 = mybir.dt.float32
F32R = mybir.dt.float32r
ALU = mybir.AluOpType
ACT = mybir.ActivationFunctionType

P = 128
BANK = 512


def rec_kernel(nc, x, W1, b1, W2, b2, out):
    B, T, S = x.shape
    O = W2.shape[0]
    JT = BANK // P
    GROUPS = B // BANK
    CW = 2
    SC = S // P
    QB = SC // CW
    BLOCKS = GROUPS * QB
    LAST = BLOCKS - 1
    APART = QB + 1
    SLOTS = 8
    RING = 4
    TURNS = SLOTS // RING
    TS = T // SLOTS
    UPS = TS * CW
    UNITS = SLOTS * UPS
    XBANKS = 6
    OH = O // BANK
    OUTS = JT * OH
    EARLY = 5
    OPEN = 8 - XBANKS
    STAGES = 4
    YS = JT
    W2_AT, W2_EVERY = 2 * UPS, 2
    H_AT, H_EVERY = XBANKS + 4, 5
    CHUNK_AT = 40
    assert B % BANK == 0 and T % SLOTS == 0 and S % (CW * P) == 0 and O == OH * BANK and OH == 2
    assert UNITS % XBANKS == 0 and SLOTS % RING == 0 and GROUPS == 2 and APART <= LAST and CW == 2
    assert W2_AT + W2_EVERY * OH * SC <= UNITS - 2 and H_AT + H_EVERY * (OUTS - 1) < UNITS - CW

    x_v = x.rearrange("(g j p) t s -> g p j t s", p=P, j=JT)
    out_v = out.rearrange("(g j p) o -> g p j o", p=P, j=JT)
    w2_v = W2.rearrange("(h j p) s -> h p j s", p=P, j=JT)
    b2_v = b2.rearrange("(a o) -> a o", a=1)

    with ExitStack() as ctx:
        def sb(name, shape, dt=F32):
            return ctx.enter_context(nc.sbuf_tensor(name, shape, dt))

        def sem(name):
            return ctx.enter_context(nc.semaphore(name))

        ring = sb("ring", [P, RING, JT, TS * CW * P])
        w_hi = sb("w_hi", [P, SC, O], F32R)
        w_lo = sb("w_lo", [P, SC, O], F32R)
        y = sb("y", [P, GROUPS * JT, O])
        b2row = sb("b2row", [1, O])
        b2all = sb("b2all", [P, O])
        ones = sb("ones", [1, P])
        acc = sb("acc", [P, CW, BANK])
        acc_odd = sb("acc_odd", [P, BANK])
        h = sb("h", [P, CW, BANK])
        h_hi = sb("h_hi", [P, CW, BANK], F32R)
        h_lo = sb("h_lo", [P, CW, BANK], F32R)
        stage = sb("stage", [P, STAGES, BANK])
        w1 = sb("w1", [P, SC * T])
        b1row = sb("b1row", [SC, P])
        b1col = sb("b1col", [P, SC])
        ident = sb("ident", [P, P])
        bank = [ctx.enter_context(nc.psum_tensor(f"bank{n}", [P, BANK], F32)) for n in range(8)]

        x_loaded = [[sem(f"x_loaded{r}_{q}") for q in range(TS)] for r in range(RING)]
        w2_loaded = [sem(f"w2_loaded{n}") for n in range(OH)]
        w1_loaded = sem("w1_loaded")
        b1_loaded = sem("b1_loaded")
        b2_loaded = sem("b2_loaded")
        ident_zeroed = sem("ident_zeroed")
        ident_ready = sem("ident_ready")
        ones_ready = sem("ones_ready")
        b1_turned = sem("b1_turned")
        b1_ready = sem("b1_ready")
        b2_spread = sem("b2_spread")
        b2_ready = sem("b2_ready")
        w2_turned = sem("w2_turned")
        w_hi_ready = sem("w_hi_ready")
        w_lo_ready = sem("w_lo_ready")
        unit_turned = sem("unit_turned")
        unit_added = sem("unit_added")
        merged = sem("merged")
        h_ready = sem("h_ready")
        h_hi_ready = sem("h_hi_ready")
        h_lo_ready = sem("h_lo_ready")
        tail_hi = sem("tail_hi")
        tail_lo = sem("tail_lo")
        out_summed = sem("out_summed")
        out_staged = sem("out_staged")
        y_written = sem("y_written")
        y_started = sem("y_started")
        y_final = sem("y_final")
        group_stored = sem("group_stored")
        stored = sem("stored")

        block = ctx.enter_context(nc.Block())

        def unit_of(apart, r, k):
            if apart:
                c, rc = divmod(r, SLOTS // CW)
                return rc * UPS + k, c, k * P
            t, c = divmod(k, CW)
            return r * TS + t, c, (t * CW + c) * P

        def chunk_seq(g):
            return APART * OUTS + (g - APART * CW) * OUTS

        def out_half(n):
            j, oh = divmod(n % OUTS, OH)
            return j, slice(oh * BANK, (oh + 1) * BANK)

        STAGED = chunk_seq(BLOCKS * CW - 1) - OPEN

        def tail_bank(n):
            return bank[XBANKS + n] if n < OPEN else bank[n - OPEN]

        @block.sync
        def _(sp):
            def load(i, r, apart=False):
                w = P if apart else CW * P
                for k in range(TS * CW * P // w):
                    t, c, col = unit_of(apart, r, k * (w // P))
                    src = x_v[i // QB, :, :, t, bass.ds(((i % QB) * CW + c) * P, w)]
                    sp.dma_start(ring[:, r % RING, :, col:col + w], src).then_inc(x_loaded[r % RING][col // (CW * P)], 16)

            for r in range(SLOTS):
                if r >= RING:
                    sp.wait_ge(unit_turned, (r - RING + 1) * UPS)
                load(0, r)
                if r in (1, 3):
                    n = r // 2
                    sp.dma_start(y[:, n * JT:(n + 1) * JT, :], w2_v[n]).then_inc(w2_loaded[n], 16)
            with sp.Fori(1, APART) as i:
                for r in range(SLOTS):
                    sp.wait_ge(unit_turned, (i * SLOTS + r - RING + 1) * UPS)
                    load(i, r)
            for i in range(APART, BLOCKS):
                for r in range(SLOTS):
                    sp.wait_ge(unit_turned, (i * SLOTS + r - RING + 1) * UPS)
                    load(i, r, apart=True)
            for n in range(OUTS):
                j, cols = out_half(n)
                sp.wait_ge(y_final, n + 1)
                sp.dma_start(out_v[GROUPS - 1][:, j, cols],
                             y[:, (GROUPS - 1) * JT + j, cols]).then_inc(stored, 16)
            sp.wait_ge(stored, 16 * OUTS)
            sp.wait_ge(group_stored, 16 * JT)

        @block.tensor
        def _(pe):
            def turn_slot(i, r, first=False, apart=False, between={}):
                loads = i * TURNS + r // RING + 1
                if apart:
                    loads += (CW - 1) * ((i - APART) * TURNS + r // RING + 1)
                for k in range(UPS):
                    u = r * UPS + k
                    _, _, col = unit_of(apart, r, k)
                    if k % CW == 0:
                        pe.wait_ge(x_loaded[r % RING][k // CW], loads * 16)
                    if not first or u >= XBANKS:
                        pe.wait_ge(unit_added, i * UNITS + u + 1 - XBANKS)
                    for j in range(JT):
                        mm = pe.transpose(bank[u % XBANKS][:, j * P:(j + 1) * P],
                                          ring[:, r % RING, j, col:col + P], ident[:, :])
                    mm.then_inc(unit_turned, 1)
                    if u in between:
                        between[u](i)

            def turn_w2(m):
                n, c = divmod(m, SC)
                pe.wait_ge(w2_loaded[n], 16)
                if m == 0:
                    pe.wait_ge(b2_ready, OH)
                if m >= 2:
                    pe.wait_ge(w_lo_ready, m - 1)
                for j in range(JT):
                    mm = pe.transpose(bank[XBANKS + m % 2][:, j * P:(j + 1) * P],
                                      y[:, n * JT + j, c * P:(c + 1) * P], ident[:, :])
                mm.then_inc(w2_turned, 1)

            def multiply(to, n, chunk, chunks, start=True, stop=True):
                j, cols = out_half(n)
                pairs = [(a, b, c) for c in chunks for a, b in ((h_hi, w_hi), (h_hi, w_lo), (h_lo, w_hi))]
                for k, (a, b, c) in enumerate(pairs):
                    mm = pe.matmul(to[:, :], a[:, c, j * P:(j + 1) * P], b[:, chunk + c, cols],
                                   start=start and k == 0, stop=stop and k == len(pairs) - 1)
                if stop:
                    mm.then_inc(out_summed, 1)

            def product(i, n):
                if n == 0:
                    pe.wait_ge(h_lo_ready, i * CW)
                if n >= 2:
                    pe.wait_ge(out_staged, (i - 1) * OUTS + n - 1)
                multiply(bank[XBANKS + n % 2], n, ((i - 1) % QB) * CW, range(CW))

            def chunk_product(g, n, start=0):
                seq = chunk_seq(g) + n - start
                if n == start:
                    pe.wait_ge(h_lo_ready, g + 1)
                pe.wait_ge(out_staged, seq - 1)
                c = g % CW
                multiply(bank[XBANKS + n % 2], n, g % SC - c, range(c, c + 1))

            pe.wait_ge(ident_ready, 1)
            def spread_biases(i):
                pe.wait_ge(b1_loaded, 16)
                pe.transpose(bank[XBANKS + 1][:, 0:SC], b1row[:, :], ident[0:SC, 0:SC]).then_inc(b1_turned, 1)
                pe.wait_ge(b2_loaded, 16)
                pe.wait_ge(ones_ready, 1)
                for n in range(OH):
                    if n == 1:
                        pe.wait_ge(b1_ready, 1)
                    pe.matmul(bank[XBANKS + n][:, :], ones[:, :], b2row[:, n * BANK:(n + 1) * BANK],
                              start=True, stop=True).then_inc(b2_spread, 1)

            spread = {W2_AT + W2_EVERY * m: lambda i, m=m: turn_w2(m) for m in range(OH * SC)}
            spread[UPS - 1] = spread_biases
            for r in range(SLOTS):
                turn_slot(0, r, first=True, between=spread)
            pe.wait_ge(w_lo_ready, OH * SC)
            spread = {H_AT + H_EVERY * n: lambda i, n=n: product(i, n) for n in range(OUTS)}
            with pe.Fori(1, APART) as i:
                for r in range(SLOTS):
                    turn_slot(i, r, between=spread)
            spread = {H_AT + 3 * n: lambda i, n=n: product(i, n) for n in range(OUTS)}
            for g in range(APART * CW, BLOCKS * CW - 2):
                at = (g - APART * CW) * (UNITS // CW) + CHUNK_AT
                for n in range(OUTS):
                    spread[at + 5 * n // 2] = lambda i, g=g, n=n: chunk_product(g, n)
            for n in range(OPEN, OUTS):
                spread[(BLOCKS - APART) * UNITS - 1 - 3 * (OUTS - 1 - n) // 2] = \
                    lambda i, n=n: chunk_product(BLOCKS * CW - 2, n, OPEN)
            for i in range(APART, BLOCKS):
                here = {u - (i - APART) * UNITS: work for u, work in spread.items()}
                for r in range(SLOTS):
                    turn_slot(i, r, apart=True, between=here)
            for n in range(OPEN):
                pe.wait_ge(out_staged, STAGED - OPEN + n + 1)
                multiply(bank[XBANKS + n], n, SC - CW, range(1), stop=False)
            for n in range(OUTS):
                pe.wait_ge(tail_lo, n // OH + 1)
                if n >= OPEN:
                    pe.wait_ge(unit_added, BLOCKS * UNITS - XBANKS + n - OPEN + 1)
                multiply(tail_bank(n), n, SC - CW, range(CW - 1, CW), start=n >= OPEN)

        @block.vector
        def _(dve):
            def add_slot(i, r, first=False, apart=False, between={}):
                for k in range(UPS):
                    u = r * UPS + k
                    t, c, _ = unit_of(apart, r, k)
                    wcol = w1[:, bass.ds(((i % QB) * CW + c) * T + t, 1)]
                    dve.wait_ge(unit_turned, i * UNITS + u + 1)
                    to = acc_odd[:, :] if apart and t % 2 else acc[:, c, :]
                    if t == 0 or apart and t == 1:
                        if t == 1 and i * CW + c > APART * CW:
                            dve.wait_ge(merged, (i - APART) * CW + c)
                        if t == 0 and not first:
                            dve.wait_ge(h_ready, (i - 1) * CW + c + 1)
                        nc.vector.tensor_scalar(to, bank[u % XBANKS][:, :], wcol, None,
                                                ALU.mult).then_inc(unit_added, 1)
                    else:
                        dve.wait_ge(unit_added, i * UNITS + u - 1)
                        nc.vector.scalar_tensor_tensor(out=to, in0=bank[u % XBANKS][:, :], scalar=wcol,
                                                       in1=to, op0=ALU.mult,
                                                       op1=ALU.add).then_inc(unit_added, 1)
                    if u in between:
                        between[u]()

            def split_w2(m):
                n, c = divmod(m, SC)
                cols = slice(n * BANK, (n + 1) * BANK)
                dve.wait_ge(w_hi_ready, m + 1)
                nc.vector.tensor_tensor(w_lo[:, c, cols], bank[XBANKS + m % 2][:, :], w_hi[:, c, cols].bitcast(F32),
                                        ALU.subtract).then_inc(w_lo_ready, 1)

            dve.wait_ge(w1_loaded, 16)
            spread = {W2_AT + W2_EVERY * m + 2: lambda m=m: split_w2(m) for m in range(OH * SC)}
            for r in range(SLOTS):
                add_slot(0, r, first=True, between=spread)
            with dve.Fori(1, APART) as i:
                for r in range(SLOTS):
                    add_slot(i, r)

            def merge(c, rows=slice(0, BANK)):
                nc.vector.tensor_tensor(acc[:, c, rows], acc[:, c, rows], acc_odd[:, rows],
                                        ALU.add).then_inc(merged, 1)

            def merge_chunk(g):
                dve.wait_ge(unit_added, APART * UNITS + (g + 1 - APART * CW) * (UNITS // CW))
                merge(g % CW)

            for i in range(APART, BLOCKS):
                spread = {UNITS // CW: lambda i=i: merge_chunk(i * CW)}
                if i > APART:
                    spread[0] = lambda i=i: merge_chunk(i * CW - 1)
                for r in range(SLOTS):
                    add_slot(i, r, apart=True, between=spread)
            dve.wait_ge(unit_added, BLOCKS * UNITS)
            for j in range(JT):
                merge(CW - 1, slice(j * P, (j + 1) * P))
            c = CW - 1
            for j in range(JT):
                rows = slice(j * P, (j + 1) * P)
                dve.wait_ge(h_ready, LAST * CW + 1 + j + 1)
                nc.vector.tensor_copy(h_hi[:, c, rows], h[:, c, rows]).then_inc(tail_hi, 1)
                dve.wait_ge(tail_hi, j + 1)
                nc.vector.tensor_tensor(h_lo[:, c, rows], h[:, c, rows], h_hi[:, c, rows].bitcast(F32),
                                        ALU.subtract).then_inc(tail_lo, 1)
            for n in range(OUTS):
                j, cols = out_half(n)
                piece = y[:, (GROUPS - 1) * JT + j, cols]
                dve.wait_ge(out_summed, STAGED + n + 1)
                dve.wait_ge(y_written, YS + STAGED - OUTS + OPEN + max(0, n - OPEN + 1))
                nc.vector.tensor_tensor(piece, tail_bank(n)[:, :], piece, ALU.add).then_inc(y_final, 1)

        @block.scalar
        def _(act):
            act.dma_start(w1[:, :].rearrange("p (c t) -> p c t", t=T),
                          W1.rearrange("(c p) t -> p c t", p=P)).then_inc(w1_loaded, 16)
            act.dma_start(b1row[:, :], b1.rearrange("(c p) -> c p", p=P)).then_inc(b1_loaded, 16)
            act.dma_start(b2row[:, :], b2_v).then_inc(b2_loaded, 16)
            act.wait_ge(b1_turned, 1)
            nc.scalar.copy(b1col[:, :], bank[XBANKS + 1][:, 0:SC]).then_inc(b1_ready, 1)
            for n in range(OH):
                act.wait_ge(b2_spread, n + 1)
                nc.scalar.copy(b2all[:, n * BANK:(n + 1) * BANK], bank[XBANKS + n][:, :]).then_inc(b2_ready, 1)
            act.wait_ge(b2_ready, OH)
            for m in range(OH * SC):
                n, c = divmod(m, SC)
                act.wait_ge(w2_turned, m + 1)
                nc.scalar.copy(w_hi[:, c, n * BANK:(n + 1) * BANK], bank[XBANKS + m % 2][:, :]).then_inc(w_hi_ready, 1)
                if SC <= m < SC + JT:
                    nc.scalar.copy(y[:, m - SC, :], b2all[:, :]).then_inc(y_written, 1)
            act.wait_ge(b1_ready, 1)

            def sigmoid(i, c, done, count, rows=slice(0, BANK)):
                act.wait_ge(done, count)
                nc.scalar.activation(h[:, c, rows], acc[:, c, rows], ACT.Sigmoid,
                                     bias=b1col[:, bass.ds((i % QB) * CW + c, 1)]).then_inc(h_ready, 1)

            def high_part(i, c):
                act.wait_ge(h_ready, i * CW + c + 1)
                nc.scalar.copy(h_hi[:, c, :], h[:, c, :]).then_inc(h_hi_ready, 1)

            def copy_piece(seq, n):
                act.wait_ge(out_summed, seq + 1)
                act.wait_ge(y_written, YS + seq - STAGES + 1)
                nc.scalar.copy(stage[:, n % STAGES, :], bank[XBANKS + n % 2][:, :]).then_inc(out_staged, 1)

            for c in range(CW):
                sigmoid(0, c, unit_added, UNITS - CW + c + 1)
            for c in range(CW):
                high_part(0, c)
            def copy_and_next_h(i):
                for n in range(OUTS):
                    copy_piece((i - 1) * OUTS + n, n)
                for c in range(CW):
                    sigmoid(i, c, unit_added, i * UNITS + UNITS - CW + c + 1)
                for c in range(CW):
                    high_part(i, c)

            with act.Fori(1, QB + 1) as i:
                copy_and_next_h(i)
            act.wait_ge(y_written, YS + QB * OUTS)

            def copy_chunk(g, pieces):
                for n in pieces:
                    copy_piece(chunk_seq(g) + n, n)

            def next_h(g):
                sigmoid(g // CW, g % CW, merged, g + 1 - APART * CW)
                high_part(g // CW, g % CW)

            for n in range(OUTS):
                copy_piece((APART - 1) * OUTS + n, n)
                if n % OH == 0:
                    act.dma_start(out_v[0][:, n // OH, :], y[:, n // OH, :]).then_inc(group_stored, 16)
            next_h(APART * CW)
            for g in range(APART * CW, BLOCKS * CW - 2):
                copy_chunk(g, range(EARLY))
                next_h(g + 1)
                copy_chunk(g, range(EARLY, OUTS))
            copy_chunk(BLOCKS * CW - 2, range(OUTS - OPEN))
            for j in range(JT):
                sigmoid(LAST, CW - 1, merged, (BLOCKS - APART) * CW - 1 + j + 1, slice(j * P, (j + 1) * P))

        @block.gpsimd
        def _(pool):
            nc.gpsimd.memset(ident[:, :], 0.0).then_inc(ident_zeroed, 1)
            pool.wait_ge(ident_zeroed, 1)
            nc.gpsimd.affine_select(out=ident[:, :], in_=ident[:, :], compare_op=ALU.not_equal, fill=1.0, base=0,
                                    pattern=[[-1, P]], channel_multiplier=1).then_inc(ident_ready, 1)
            nc.gpsimd.memset(ones[:, :], 1.0).then_inc(ones_ready, 1)
            def low_part(i, c):
                pool.wait_ge(h_hi_ready, i * CW + c + 1)
                nc.gpsimd.tensor_tensor(h_lo[:, c, :], h[:, c, :], h_hi[:, c, :].bitcast(F32),
                                        ALU.subtract).then_inc(h_lo_ready, 1)

            def add_pieces(g, seq, pieces=range(OUTS), at=0, between={}):
                pool.wait_ge(y_written, YS + seq)
                for k, n in enumerate(pieces):
                    j, cols = out_half(n)
                    piece = y[:, g * JT + j, cols]
                    pool.wait_ge(out_staged, seq + k + 1)
                    nc.gpsimd.tensor_tensor(piece, stage[:, (at + k) % STAGES, :], piece,
                                            ALU.add).then_inc(y_written, 1)
                    if n in between:
                        between[n]()

            def start_tile(k):
                nc.gpsimd.tensor_copy(y[:, JT + k, :], b2all[:, :]).then_inc(y_started, 1)

            for c in range(CW):
                low_part(0, c)
            pool.wait_ge(b2_ready, OH)
            pool.wait_ge(w2_turned, OH * SC)
            add_pieces(0, 0, between={n: lambda n=n: start_tile(n) for n in range(JT)})
            with pool.Fori(1, QB) as i:
                for c in range(CW):
                    low_part(i, c)
                add_pieces(0, i * OUTS)
            pool.wait_ge(y_started, JT)
            with pool.Fori(QB, APART) as i:
                for c in range(CW):
                    low_part(i, c)
                add_pieces(1, i * OUTS)
            low_part(APART, 0)
            for g in range(APART * CW, BLOCKS * CW - 2):
                add_pieces(1, chunk_seq(g), range(EARLY))
                low_part((g + 1) // CW, (g + 1) % CW)
                add_pieces(1, chunk_seq(g) + EARLY, range(EARLY, OUTS), at=EARLY % STAGES)
            add_pieces(1, chunk_seq(BLOCKS * CW - 2), range(OPEN, OUTS))


_INS = ["r_x", "L0_rec_W1", "L0_rec_b1", "L0_rec_W2", "L0_rec_b2"]


def kernel(**inputs):
    import numpy as np
    import concourse.bacc as bacc
    from concourse.bass_utils import run_bass_kernel_spmd as run

    nc = bacc.Bacc("TRN2", target_bir_lowering=False, num_devices=1)
    arrays, args = {}, []
    for name in _INS:
        a = np.ascontiguousarray(inputs[name])
        arrays[f"in_{name}"] = a
        args.append(nc.dram_tensor(f"in_{name}", a.shape, mybir.dt.from_np(a.dtype), kind="ExternalInput").ap())
    rows, cols = inputs["r_x"].shape[0], inputs["L0_rec_W2"].shape[0]
    args.append(nc.dram_tensor("out_y", (rows, cols), F32, kind="ExternalOutput").ap())
    rec_kernel(nc, *args)
    r = run(nc, [arrays], core_ids=[0])
    return r.results[0]["out_y"]
```
